# Optimizing a Trainium2 kernel written in Bass

```python
import numpy as np
import jax
import jax.numpy as jnp

def _softmax(x, axis=-1):
    return jax.nn.softmax(x, axis=axis)

def _gelu(x):
    return jax.nn.gelu(x, approximate=True)

def _silu(x):
    return jax.nn.silu(x)

def _sigmoid(x):
    return jax.nn.sigmoid(x)

def _layernorm(x, axis=-1, eps=1e-05):
    m = jnp.mean(x, axis=axis, keepdims=True)
    v = jnp.var(x, axis=axis, keepdims=True)
    return (x - m) / jnp.sqrt(v + eps)

def _scatter_add(tgt, idx, src, axis=0):
    return tgt.at[idx].add(src)

def _segment_sum(src, seg, n):
    return jax.ops.segment_sum(src, seg, n)
kernel_name = 'mk_cond_resid_d4_seqx_r4_77dd00'

def setup_inputs(seed: int=0):
    np.random.seed(seed)
    _w = jnp.asarray

    def _rec_inputs():
        import jax
        import jax.numpy as jnp
        _rk = jax.random.key(seed)
        x = -0.000125 + 0.9999 * jax.random.normal(jax.random.fold_in(_rk, 1), (8, 256, 1024), jnp.float32)
        _lenS = 256 - jax.random.randint(jax.random.fold_in(_rk, 7), (8,), 0, max(1, 256 // 4) + 1, jnp.int32)
        _lenS2 = 256 - jax.random.randint(jax.random.fold_in(_rk, 8), (8,), 0, max(1, 256 // 4) + 1, jnp.int32)
        itok_B_0_7 = jax.random.randint(jax.random.fold_in(_rk, 11), (8,), 0, 8, jnp.int32)
        condB_coeff = 0.00219231 + 0.0100837 * jax.random.normal(jax.random.fold_in(_rk, 12), (8,), jnp.float32)
        itok_B_3_7 = jax.random.randint(jax.random.fold_in(_rk, 14), (8,), 3, 8, jnp.int32)
        _validS = jnp.arange(256)[None, :] < _lenS[:, None]
        _validS2 = jnp.arange(256)[None, :] < _lenS2[:, None]
        _causal = jnp.tril(jnp.ones((256, 256), dtype=bool))
        mask_Bx4096x4096_ik1 = jnp.where(jnp.ones((8, 1024, 1024), dtype=bool), 1, 0).astype(jnp.int32)
        return (x, itok_B_0_7, condB_coeff, itok_B_3_7, mask_Bx4096x4096_ik1)
    x, itok_B_0_7, condB_coeff, itok_B_3_7, mask_Bx4096x4096_ik1 = _rec_inputs()

    def _L0_cond_setup():
        import jax, jax.numpy as jnp
        import numpy as np
        TOP_K = 2
        LANG_BIAS = 5.0
        SCALING = 32.0 / 16.0
        LANGUAGE_PAD_ID = -1
        key = jax.random.key(seed)
        ks = jax.random.split(key, 6)
        B, T, D, O, E, R = (4, 512, 1024, 1024, 8, 16)
        x = jax.random.normal(ks[0], (B, T, D), dtype=jnp.float32)
        language_ids = jax.random.randint(ks[1], (B,), 0, E).astype(jnp.int64)
        W = jax.random.normal(ks[2], (O, D), dtype=jnp.float32) * (1.0 / np.sqrt(D))
        Wr = jax.random.normal(ks[3], (E, D), dtype=jnp.float32) * (1.0 / np.sqrt(D))
        A = jax.random.normal(ks[4], (E, R, D), dtype=jnp.float32) * (1.0 / np.sqrt(D))
        Bm = jax.random.normal(ks[5], (O, R), dtype=jnp.float32) * 0.0
        Bm = jnp.broadcast_to(Bm, (E, O, R)) + jax.random.normal(ks[5], (E, O, R), dtype=jnp.float32) * 0.02
        return {'x': x, 'language_ids': language_ids, 'W': W, 'Wr': Wr, 'A': A, 'B': Bm}
    _L0_cond_all = _L0_cond_setup()
    _L0_cond_in = {k: v for k, v in _L0_cond_all.items() if k in ('W', 'Wr', 'A', 'B')}
    del _L0_cond_all

    def _L1_cond_setup():
        import jax, jax.numpy as jnp
        import numpy as np
        B, S, D_IN, D_OUT = (4, 128, 1024, 1024)
        key = jax.random.key(seed)
        k1, k2, k3, k4, k5 = jax.random.split(key, 5)
        hidden_states = jax.random.normal(k1, (B, S, D_IN), dtype=jnp.float32)
        W = jax.random.normal(k2, (D_OUT, D_IN), dtype=jnp.float32) * 0.02
        b = jax.random.normal(k3, (D_OUT,), dtype=jnp.float32) * 0.02
        coeff = jax.random.normal(k4, (B,), dtype=jnp.float32) * 0.01
        mask = jax.random.randint(k5, (B, D_IN, D_OUT), 0, 2, dtype=jnp.int32)
        return {'hidden_states': hidden_states, 'W': W, 'b': b, 'coeff': coeff, 'mask': mask}
    _L1_cond_all = _L1_cond_setup()
    _L1_cond_in = {k: v for k, v in _L1_cond_all.items() if k in ('W', 'b')}
    del _L1_cond_all

    def _L2_cond_setup():
        import jax, jax.numpy as jnp
        import numpy as np
        MAX_LORAS, OUT, IN = (8, 1024, 1024)
        B, S = (4, 512)
        key = jax.random.key(seed)
        k1, k2, k3 = jax.random.split(key, 3)
        x = jax.random.normal(k1, (B, S, IN), dtype=jnp.float32)
        weight = jax.random.normal(k2, (MAX_LORAS, OUT, IN), dtype=jnp.float32) * 0.02
        adapter_ids = jax.random.randint(k3, (B,), 0, MAX_LORAS, dtype=jnp.int32)
        return {'x': x, 'weight': weight, 'adapter_ids': adapter_ids}
    _L2_cond_all = _L2_cond_setup()
    _L2_cond_in = {k: v for k, v in _L2_cond_all.items() if k in ('weight',)}
    del _L2_cond_all

    def _L3_cond_setup():
        import jax, jax.numpy as jnp
        import numpy as np
        RANK = 16
        ALPHA = 16.0
        SCALING = ALPHA / RANK
        N_ADAPTERS = 8
        IN_F = 1024
        OUT_F = 1024
        BATCH = 4
        SEQ = 512
        key = jax.random.key(seed)
        kx, ka, kb, ki = jax.random.split(key, 4)
        x = jax.random.normal(kx, (BATCH, SEQ, IN_F), dtype=jnp.float32)
        A = jax.random.normal(ka, (N_ADAPTERS, OUT_F, RANK), dtype=jnp.float32) * 0.02
        B = jax.random.normal(kb, (N_ADAPTERS, RANK, IN_F), dtype=jnp.float32) * 0.02
        adapter_ids = jax.random.randint(ki, (BATCH,), 0, N_ADAPTERS, dtype=jnp.int32)
        return {'x': x, 'A': A, 'B': B, 'adapter_ids': adapter_ids}
    _L3_cond_all = _L3_cond_setup()
    _L3_cond_in = {k: v for k, v in _L3_cond_all.items() if k in ('A', 'B')}
    del _L3_cond_all
    return {'x': x, 'itok_B_0_7': itok_B_0_7, 'condB_coeff': condB_coeff, 'itok_B_3_7': itok_B_3_7, 'mask_Bx4096x4096_ik1': mask_Bx4096x4096_ik1, 'L0_cond_W': _L0_cond_in['W'], 'L0_cond_Wr': _L0_cond_in['Wr'], 'L0_cond_A': _L0_cond_in['A'], 'L0_cond_B': _L0_cond_in['B'], 'L1_cond_W': _L1_cond_in['W'], 'L1_cond_b': _L1_cond_in['b'], 'L2_cond_weight': _L2_cond_in['weight'], 'L3_cond_A': _L3_cond_in['A'], 'L3_cond_B': _L3_cond_in['B']}

def reference(x, itok_B_0_7, condB_coeff, itok_B_3_7, mask_Bx4096x4096_ik1, L0_cond_W, L0_cond_Wr, L0_cond_A, L0_cond_B, L1_cond_W, L1_cond_b, L2_cond_weight, L3_cond_A, L3_cond_B):
    import jax
    import jax.numpy as jnp

    def _L0_cond_ref(x, language_ids, W, Wr, A, B):
        import jax, jax.numpy as jnp
        import numpy as np
        TOP_K = 2
        LANG_BIAS = 5.0
        SCALING = 32.0 / 16.0
        LANGUAGE_PAD_ID = -1
        base = jnp.einsum('btd,od->bto', x, W)
        E = Wr.shape[0]
        logits = jnp.einsum('btd,ed->bte', x.astype(jnp.float32), Wr.astype(jnp.float32))
        expert_targets = language_ids
        valid = expert_targets >= 0
        tgt = jnp.where(valid, expert_targets, 0)
        bias = jax.nn.one_hot(tgt, E, dtype=logits.dtype) * LANG_BIAS
        bias = jnp.where(valid[:, None], bias, 0.0)
        logits = logits + bias[:, None, :]
        topw, topi = jax.lax.top_k(logits, TOP_K)
        weights = jax.nn.softmax(topw, axis=-1)
        gates = jnp.sum(jax.nn.one_hot(topi, E, dtype=weights.dtype) * weights[..., None], axis=-2)
        gates = gates.astype(x.dtype)
        h = jnp.einsum('btd,erd->bter', x, A)
        lora_out = jnp.einsum('bter,bte,eor->bto', h, gates, B)
        return base + SCALING * lora_out

    def _L1_cond_ref(hidden_states, W, b, coeff, mask):
        import jax, jax.numpy as jnp
        import numpy as np
        B, S, D_IN, D_OUT = (4, 128, 1024, 1024)
        output = jnp.einsum('bsi,oi->bso', hidden_states, W) + b
        sign = (2 * mask - 1).astype(hidden_states.dtype)
        diff = jnp.einsum('bsi,bio->bso', hidden_states, sign)
        return output + diff * coeff[:, None, None]

    def _L2_cond_ref(x, weight, adapter_ids):
        import jax, jax.numpy as jnp
        import numpy as np
        MAX_LORAS, OUT, IN = (8, 1024, 1024)
        B, S = (4, 512)
        w = weight[adapter_ids]
        return jnp.einsum('bsi,boi->bso', x, w)

    def _L3_cond_ref(x, A, B, adapter_ids):
        import jax, jax.numpy as jnp
        import numpy as np
        RANK = 16
        ALPHA = 16.0
        SCALING = ALPHA / RANK
        N_ADAPTERS = 8
        IN_F = 1024
        OUT_F = 1024
        BATCH = 4
        SEQ = 512
        B_sel = B[adapter_ids]
        A_sel = A[adapter_ids]
        Bx = jnp.einsum('bni,bri->bnr', x, B_sel)
        out = jnp.einsum('bnr,bor->bno', Bx, A_sel)
        return out * SCALING
    x = x + _L0_cond_ref(x, itok_B_0_7, L0_cond_W, L0_cond_Wr, L0_cond_A, L0_cond_B)
    x = x + _L1_cond_ref(x, L1_cond_W, L1_cond_b, condB_coeff, mask_Bx4096x4096_ik1)
    x = x + _L2_cond_ref(x, L2_cond_weight, itok_B_3_7)
    x = x + _L3_cond_ref(x, L3_cond_A, L3_cond_B, itok_B_3_7)
    return x

_drawn_inputs = setup_inputs


def setup_inputs(seed=0):
    import zlib

    import numpy as np

    out = dict(_drawn_inputs(seed))
    spreads = {}
    factors = {'L0_cond_Wr': 5.191, 'L1_cond_b': 4.983}
    for name, (base, spread) in spreads.items():
        noise = np.random.default_rng([zlib.crc32(name.encode()), seed]).standard_normal(out[name].shape)
        drawn = base * np.exp(spread * noise) if base else spread * noise
        out[name] = jnp.asarray(drawn.astype(out[name].dtype))
    for name, factor in factors.items():
        out[name] = (out[name] * factor).astype(out[name].dtype)
    return out
```

```python
from contextlib import ExitStack

import concourse.bass as bass
from concourse import mybir

P = 128
BATCHES = 8
TOKENS = 256
D = 1024
KT = D // P
OT = D // P
PAIRS = OT // 2
TT = TOKENS // P
EXPERTS = 8
RANK = 16
ER = EXPERTS * RANK
HL = ER + EXPERTS
LANG_BIAS = 5.0
SCALING = 2.0
LOWEST = -3.0e38
RING = 6
AHEAD = 3
PER_ITER = 18
FIRST = 4
REP = 3
ROWS3 = REP * 2 * RANK

F32 = mybir.dt.float32
F32R = mybir.dt.float32r
I32 = mybir.dt.int32
ALU = mybir.AluOpType
ACT = mybir.ActivationFunctionType
AX_X = mybir.AxisListType.X

CHUNKS = list(range(14)) + [("x", 0), 14, ("x", 1), 15]
X_HALVES = [("x", 0), ("x", 1)]
L0_BANK = [6, 7, 0, 1]
L1_BANK = [6, 7, 6, 7]
L2_BANK = [2, 3, 0, 1]
GATE_STEPS = 20


def cond_resid_kernel(nc, x, lang_ids, coeff, ids, mask, w0, wr, a0, b0, w1, bias1, w2, a3, b3, out):
    ctx = ExitStack()
    with ctx:
        def sb(name, shape, dt=F32):
            return ctx.enter_context(nc.sbuf_tensor(name, shape, dt))

        def sem(name):
            return ctx.enter_context(nc.semaphore(name))

        w0_hi = sb("w0_hi", [P, OT, KT, P], F32R)
        w0_lo = sb("w0_lo", [P, OT, KT, P], F32R)
        w1_full = sb("w1_full", [P, OT, KT, P])
        awr_hi = sb("awr_hi", [P, KT, HL], F32R)
        awr_lo = sb("awr_lo", [P, KT, HL], F32R)
        b0_hi = sb("b0_hi", [P, D], F32R)
        b0_lo = sb("b0_lo", [P, D], F32R)
        raw = sb("raw", [P, RING, KT, P])
        hi_ring = sb("hi_ring", [P, 2, KT, P], F32R)
        lo_ring = sb("lo_ring", [P, 2, KT, P], F32R)
        in03_hi = sb("in03_hi", [P, KT, TOKENS], F32R)
        in03_lo = sb("in03_lo", [P, KT, TOKENS], F32R)
        in1_hi = sb("in1_hi", [P, KT, TOKENS], F32R)
        in1_lo = sb("in1_lo", [P, KT, TOKENS], F32R)
        in2_hi = sb("in2_hi", [P, KT, TOKENS], F32R)
        in2_lo = sb("in2_lo", [P, KT, TOKENS], F32R)
        gated = sb("gated", [P, TT, ER])
        gatedT_hi = sb("gatedT_hi", [P, TOKENS], F32R)
        gatedT_lo = sb("gatedT_lo", [P, TOKENS], F32R)
        logits = sb("logits", [P, TT, EXPERTS])
        rest = sb("rest", [P, TT, EXPERTS])
        same = sb("same", [P, TT, EXPERTS])
        key = sb("key", [P, TT, EXPERTS])
        pick1 = sb("pick1", [P, TT, EXPERTS])
        pick2 = sb("pick2", [P, TT, EXPERTS])
        gates_sb = sb("gates_sb", [P, TT, EXPERTS])
        stat = sb("stat", [P, 8, TT])
        a3_raw = sb("a3_raw", [ROWS3, D])
        a3_split = sb("a3_split", [ROWS3, D], F32R)
        b3_raw = sb("b3_raw", [P, KT, RANK])
        b3_split = sb("b3_split", [P, KT, REP, 2, RANK], F32R)
        rank_rows = sb("rank_rows", [ROWS3, TOKENS], F32R)
        stage = sb("stage", [P, 2, 2 * TOKENS])
        ident = sb("ident", [P, P])
        first_key = sb("first_key", [P, EXPERTS])
        expert_no = sb("expert_no", [P, EXPERTS])
        expert_i = sb("expert_i", [P, EXPERTS], I32)
        lang_i = sb("lang_i", [P, BATCHES], I32)
        lang_f = sb("lang_f", [P, BATCHES])
        lang_bias = sb("lang_bias", [P, BATCHES, EXPERTS])
        ids_row = sb("ids_row", [1, BATCHES], I32)
        coeff_all = sb("coeff_all", [P, BATCHES])
        coeff_pair = sb("coeff_pair", [P, BATCHES, 2])
        coeff_now = sb("coeff_now", [P, 2])
        wr_raw = sb("wr_raw", [P, KT, EXPERTS])
        bias_sb = sb("bias_sb", [P, OT])
        bank = [ctx.enter_context(nc.psum_tensor(f"bank{i}", [P, 2 * TOKENS], F32)) for i in range(8)]
        down = bank[4][:, 0:TT * HL].rearrange("p (s c) -> p s c", s=TT)
        gatedT_ps = bank[5][:, 0:TOKENS]
        rank_ps = bank[5][0:ROWS3, TOKENS:2 * TOKENS]

        raw_landed = [sem(f"raw_landed{s}") for s in range(RING)]
        w1_landed = [sem(f"w1_landed{i}") for i in range(OT)]
        wr_landed = sem("wr_landed")
        small_landed, ids_landed = sem("small_landed"), sem("ids_landed")
        a3_landed, b3_landed = sem("a3_landed"), sem("b3_landed")
        out_stored = [sem("out_stored0"), sem("out_stored1")]
        zeroed, consts_ready, setup_step = sem("zeroed"), sem("consts_ready"), sem("setup_step")
        awr_hi_ready, awr_lo_ready = sem("awr_hi_ready"), sem("awr_lo_ready")
        b0_hi_ready, b0_lo_ready = sem("b0_hi_ready"), sem("b0_lo_ready")
        w1_diag, coeff_ready = sem("w1_diag"), sem("coeff_ready")
        sign_ready, full_ready = sem("sign_ready"), sem("full_ready")
        hi_ready, lo_ready = sem("hi_ready"), sem("lo_ready")
        hi_used, tile_done = sem("hi_used"), sem("tile_done")
        x_hi_ready, x_lo_ready = sem("x_hi_ready"), sem("x_lo_ready")
        down_done, gate_step, exp_ready = sem("down_done"), sem("gate_step"), sem("exp_ready")
        gated_ready, gatedT_done = sem("gated_ready"), sem("gatedT_done")
        gatedT_hi_ready, gatedT_lo_ready = sem("gatedT_hi_ready"), sem("gatedT_lo_ready")
        l0_done = sem("l0_done")
        in1_hi_ready, in1_lo_ready = sem("in1_hi_ready"), sem("in1_lo_ready")
        in2_hi_ready, in2_lo_ready = sem("in2_hi_ready"), sem("in2_lo_ready")
        in3_hi_ready, in3_lo_ready = sem("in3_hi_ready"), sem("in3_lo_ready")
        a3_hi_ready, a3_ready = sem("a3_hi_ready"), sem("a3_ready")
        b3_hi_ready, b3_ready = sem("b3_hi_ready"), sem("b3_ready")
        rank_done, rank_hi_ready, rank_ready = sem("rank_done"), sem("rank_hi_ready"), sem("rank_ready")
        l3_done, staged = sem("l3_done"), sem("staged")

        block = ctx.enter_context(nc.Block())

        def slot_of(j):
            return (FIRST + j) % RING

        def loads_of(t, j):
            return 16 * (t * (PER_ITER // RING) + (FIRST + j) // RING + 1)

        @block.sync
        def _(sp):
            def free_slot(t, j):
                tt = t if j >= RING else t - 1
                before = CHUNKS[(j - RING) % PER_ITER]
                if before in X_HALVES:
                    sp.wait_ge(x_lo_ready, 2 * (tt + 1) + before[1] + 1)
                else:
                    sp.wait_ge(lo_ready, 16 * tt + before + 1)

            def load_raw(slot, src, dtype=F32):
                dst = raw[:, slot, :, :].rearrange("p k c -> p (k c)")
                sp.dma_start(dst if dtype == F32 else dst.bitcast(dtype), src).then_inc(raw_landed[slot], 16)

            def load_x(batch, half, slot):
                load_raw(slot, x[bass.ds(batch, 1), half, :, :].rearrange("b p c -> (b p) c"))

            def load_chunk(t, j, expert):
                c, slot = CHUNKS[j], slot_of(j)
                if c in X_HALVES:
                    load_x((t + 1) % BATCHES, c[1], slot)
                elif c >= OT:
                    load_raw(slot, mask[bass.ds(t, 1), c - OT, :, :].rearrange("b p c -> (b p) c"), I32)
                elif expert is None:
                    load_raw(slot, w0[c])
                else:
                    load_raw(slot, w2[bass.ds(expert, 1), c, :, :].rearrange("e p c -> (e p) c"))

            def id_of(t):
                return sp.value_load(ids_row[0:1, bass.ds(t, 1)], min_val=0, max_val=EXPERTS - 1)

            def load_layer3(t):
                expert = id_of(t)
                for r in range(2 * REP):
                    sp.dma_start(a3_raw[RANK * r:RANK * (r + 1), :],
                                 a3[bass.ds(expert, 1), :, :].rearrange("e r o -> (e r) o")
                                 ).then_inc(a3_landed, 16)
                sp.dma_start(b3_raw[:, :, :].rearrange("p k r -> p (k r)"),
                             b3[bass.ds(expert, 1), :, :].rearrange("e p c -> (e p) c")
                             ).then_inc(b3_landed, 16)

            for half in range(2):
                load_raw(half, x[0, half])
            load_raw(2, a0)
            sp.dma_start(wr_raw[:, :, :].rearrange("p k e -> p (k e)"), wr).then_inc(wr_landed, 16)
            load_raw(3, b0)
            load_raw(slot_of(0), w0[0])
            sp.dma_start(lang_i[:, :], lang_ids.partition_broadcast(P)).then_inc(small_landed, 16)
            sp.dma_start(coeff_all[:, :], coeff.partition_broadcast(P)).then_inc(small_landed, 16)
            sp.dma_start(bias_sb[:, :], bias1).then_inc(small_landed, 16)
            sp.dma_start(ids_row[:, :], ids.partition_broadcast(1)).then_inc(ids_landed, 16)
            load_raw(slot_of(1), w0[1])
            for j in range(2, PER_ITER):
                if j >= RING:
                    free_slot(0, j)
                elif j == 5:
                    sp.wait_ge(b0_lo_ready, 1)
                elif j == 4:
                    sp.wait_ge(awr_lo_ready, 1)
                else:
                    sp.wait_ge(x_lo_ready, j - 1)
                load_chunk(0, j, None)
                if CHUNKS[j] in range(OT - 2, 2 * OT - 2):
                    i = CHUNKS[j] - (OT - 2)
                    sp.dma_start(w1_full[:, i, :, :].rearrange("p k c -> p (k c)"), w1[i]
                                 ).then_inc(w1_landed[i], 16)
            sp.wait_ge(ids_landed, 16)
            load_layer3(0)

            with sp.Fori(1, BATCHES) as t:
                expert = id_of(t - 1)
                for j in range(PER_ITER):
                    free_slot(t, j)
                    load_chunk(t, j, expert)
                sp.wait_ge(a3_ready, t)
                sp.wait_ge(b3_ready, t)
                load_layer3(t)

            expert = id_of(BATCHES - 1)
            for j in range(OT):
                free_slot(BATCHES, j)
                load_chunk(BATCHES, j, expert)

        @block.gpsimd
        def _(pool):
            pool.iota(expert_i[:, :], [[1, EXPERTS]], base=0, channel_multiplier=0).then_inc(zeroed, 1)
            pool.memset(ident[:, :], 0.0).then_inc(zeroed, 1)
            pool.wait_ge(zeroed, 2)
            pool.affine_select(out=ident[:, :], in_=ident[:, :], compare_op=ALU.not_equal, fill=1.0,
                               base=0, pattern=[[-1, P]], channel_multiplier=1).then_inc(consts_ready, 1)

        @block.tensor
        def _(pe):
            def product(o, parts, first, last, done=None):
                for n, (w, v) in enumerate(parts):
                    mm = pe.matmul(o, w, v, start=first and n == 0, stop=last and n == len(parts) - 1,
                                   skip_group_check=True)
                if done is not None:
                    mm.then_inc(done, 1)

            def half_of(b, i):
                return bank[b][:, (i % 2) * TOKENS:(i % 2 + 1) * TOKENS]

            def down_projections(t):
                pe.wait_ge(x_lo_ready, 2 * t + 2)
                for s in range(TT):
                    tok = slice(s * P, (s + 1) * P)
                    parts = []
                    for k in range(KT):
                        parts += [(in03_hi[:, k, tok], awr_hi[:, k, :]), (in03_hi[:, k, tok], awr_lo[:, k, :]),
                                  (in03_lo[:, k, tok], awr_hi[:, k, :])]
                    product(down[:, s, :], parts, s == 0, True, down_done if s == TT - 1 else None)

            def base0(t, i):
                if isinstance(t, int):
                    pe.wait_ge(lo_ready, i + 1)
                parts = []
                for k in range(KT):
                    parts += [(w0_hi[:, i, k, :], in03_hi[:, k, :]), (w0_hi[:, i, k, :], in03_lo[:, k, :])]
                for k in range(KT):
                    parts += [(w0_lo[:, i, k, :], in03_hi[:, k, :])]
                product(half_of(L0_BANK[i // 2], i), parts, i % 2 == 0, False)

            def turn_gated(t):
                pe.wait_ge(gated_ready, t + 1)
                for s in range(TT):
                    mm = pe.transpose(gatedT_ps[:, s * P:(s + 1) * P], gated[:, s, :], ident[:, :])
                mm.then_inc(gatedT_done, 1)

            def up0(t, i):
                cols = slice(i * P, (i + 1) * P)
                product(half_of(L0_BANK[i // 2], i),
                        [(b0_hi[:, cols], gatedT_hi[:, :]), (b0_hi[:, cols], gatedT_lo[:, :]),
                         (b0_lo[:, cols], gatedT_hi[:, :])], False, True, l0_done)

            def layer0(t):
                down_projections(t)
                for i in range(3):
                    if not isinstance(t, int) and i % 2 == 0:
                        pe.wait_ge(in2_lo_ready, 8 * (t - 1) + 6 + i)
                    base0(t, i)
                turn_gated(t)
                base0(t, 3)
                pe.wait_ge(gatedT_lo_ready, t + 1)
                for i in range(4):
                    up0(t, i)
                for i in range(4, OT):
                    base0(t, i)
                    up0(t, i)

            def streamed(t, q, banks, in_hi, in_lo, in_ready):
                i, slot = q % OT, q % 2
                o = half_of(banks[i // 2], i)
                pe.wait_ge(hi_ready, 16 * t + q + 1)
                for k in range(KT):
                    if i == 0:
                        in_ready(k)
                    product(o, [(hi_ring[:, slot, k, :], in_hi[:, k, :]), (hi_ring[:, slot, k, :], in_lo[:, k, :])],
                            i % 2 == 0 and k == 0, False, hi_used if k == KT - 1 else None)
                pe.wait_ge(lo_ready, 16 * t + q + 1)
                product(o, [(lo_ring[:, slot, k, :], in_hi[:, k, :]) for k in range(KT)], False, True, tile_done)

            def layer1(t, i):
                def in_ready(k):
                    if k % 2 == 0:
                        pe.wait_ge(in1_lo_ready, 4 * t + k // 2 + 1)
                if i in (4, 6):
                    pe.wait_ge(in2_lo_ready, 8 * t + i - 2)
                streamed(t, OT + i, L1_BANK, in1_hi, in1_lo, in_ready)

            def layer2(t, i):
                streamed(t, i, L2_BANK, in2_hi, in2_lo,
                         lambda k: pe.wait_ge(in2_lo_ready, 8 * (t - 1) + k + 1))

            def layer3_rank(t):
                pe.wait_ge(b3_ready, t)
                for k in range(KT):
                    if k % 2 == 0:
                        pe.wait_ge(in3_lo_ready, 4 * (t - 1) + k // 2 + 1)
                    w = b3_split[:, k, :, :, :].rearrange("p a b c -> p (a b c)")
                    product(rank_ps, [(w, in03_hi[:, k, :]), (w, in03_lo[:, k, :])],
                            k == 0, k == KT - 1, rank_done if k == KT - 1 else None)

            def layer3_up(t):
                pe.wait_ge(a3_ready, t)
                pe.wait_ge(rank_ready, t)
                for i in range(OT):
                    product(half_of(L2_BANK[i // 2], i),
                            [(a3_split[:, i * P:(i + 1) * P], rank_rows[:, :])],
                            False, True, l3_done if i % 2 else None)

            pe.wait_ge(awr_lo_ready, 1)
            pe.wait_ge(b0_lo_ready, 1)
            pe.wait_ge(consts_ready, 1)
            layer0(0)
            for i in range(OT):
                layer1(0, i)

            with pe.Fori(1, BATCHES) as t:
                layer0(t)
                for i in range(OT):
                    layer2(t, i)
                layer1(t, 0)
                layer3_rank(t)
                layer1(t, 1)
                layer3_up(t)
                for i in range(2, OT):
                    layer1(t, i)

            for i in range(OT):
                layer2(BATCHES, i)
            layer3_rank(BATCHES)
            layer3_up(BATCHES)

        @block.scalar
        def _(act):
            def finish_raw(t, q):
                if not OT <= q < 2 * OT:
                    return
                j = CHUNKS.index(q)
                tile = raw[:, slot_of(j), :, :].rearrange("p k c -> p (k c)")
                if q == OT:
                    act.wait_ge(coeff_ready, t + 1)
                act.wait_ge(raw_landed[slot_of(j)], loads_of(t, j))
                act.activation(tile, tile.bitcast(I32), ACT.Identity, bias=coeff_now[:, 1:2],
                               scale=coeff_now[:, 0:1]).then_inc(sign_ready, 1)

            def split_tile(t, q, last=False):
                if not last:
                    finish_raw(t, q + AHEAD)
                j = CHUNKS.index(q % (2 * OT))
                act.wait_ge(full_ready, 16 * t + q + 1)
                if isinstance(t, int) and t == 0 and q < OT:
                    dst = w0_hi[:, q, :, :]
                else:
                    dst = hi_ring[:, q % 2, :, :]
                    if not (isinstance(t, int) and t == 0 and q < OT + 2):
                        act.wait_ge(hi_used, 16 * t + q - 9)
                        act.wait_ge(lo_ready, 16 * t + q - 1)
                act.activation(dst, raw[:, slot_of(j), :, :], ACT.Copy).then_inc(hi_ready, 1)

            def split_x(t, half):
                j = CHUNKS.index(("x", half))
                act.wait_ge(raw_landed[slot_of(j)], loads_of(t, j))
                act.activation(in03_hi[:, 4 * half:4 * half + 4, :].rearrange("p k c -> p (k c)"),
                               raw[:, slot_of(j), :, :].rearrange("p k c -> p (k c)"),
                               ACT.Copy).then_inc(x_hi_ready, 1)

            def evacuate0(t, p):
                act.wait_ge(l0_done, 8 * t + 2 * p + 2)
                act.activation(in1_hi[:, 2 * p:2 * p + 2, :].rearrange("p k c -> p (k c)"),
                               bank[L0_BANK[p]][:, :], ACT.Copy).then_inc(in1_hi_ready, 1)

            def evacuate1(t, p):
                act.wait_ge(tile_done, 16 * t + 2 * p + 2)
                for i in (2 * p, 2 * p + 1):
                    act.activation(in2_hi[:, i, :], bank[L1_BANK[p]][:, (i % 2) * TOKENS:(i % 2 + 1) * TOKENS],
                                   ACT.Identity, bias=bias_sb[:, i:i + 1]).then_inc(in2_hi_ready, 1)

            def evacuate2(t, p):
                act.wait_ge(tile_done, 16 * t + 2 * p - 6)
                act.activation(in03_hi[:, 2 * p:2 * p + 2, :].rearrange("p k c -> p (k c)"),
                               bank[L2_BANK[p]][:, :], ACT.Copy).then_inc(in3_hi_ready, 1)

            def gates(t):
                act.wait_ge(gate_step, GATE_STEPS * t + 9)
                act.activation(stat[:, 5, :], stat[:, 4, :], ACT.Exp).then_inc(exp_ready, 1)

            def split_gated(t):
                act.wait_ge(gatedT_done, t + 1)
                act.activation(gatedT_hi[:, :], gatedT_ps, ACT.Copy).then_inc(gatedT_hi_ready, 1)

            def split_layer3(t):
                act.wait_ge(b3_landed, 16 * t)
                for r in range(REP):
                    op = act.activation(b3_split[:, :, r, 0, :], b3_raw[:, :, :], ACT.Copy)
                op.then_inc(b3_hi_ready, 1)
                act.wait_ge(a3_landed, 16 * 2 * REP * t)
                act.activation(a3_split[:, :], a3_raw[:, :], ACT.Copy).then_inc(a3_hi_ready, 1)

            def split_rank(t):
                act.wait_ge(rank_done, t)
                act.activation(rank_rows[:, :], rank_ps, ACT.Copy).then_inc(rank_hi_ready, 1)

            def store(t, p):
                if p >= 2:
                    act.wait_ge(out_stored[p % 2], 16 * (2 * (t - 1) + 1))
                act.wait_ge(l3_done, 4 * (t - 1) + p + 1)
                act.activation(stage[:, p % 2, :], bank[L2_BANK[p]][:, :], ACT.Copy).then_inc(staged, 1)
                act.wait_ge(staged, 4 * (t - 1) + p + 1)
                act.dma_start(out[bass.ds(t - 1, 1), p, :, :].rearrange("b p c -> (b p) c"),
                              stage[:, p % 2, :]).then_inc(out_stored[p % 2], 16)

            def all_stored(t):
                for s in range(2):
                    act.wait_ge(out_stored[s], 16 * 2 * t)

            def layer1_phase(t, rest):
                split_tile(t, 10)
                if rest:
                    split_rank(t)
                split_tile(t, 11)
                evacuate1(t, 0)
                if rest:
                    store(t, 0)
                    store(t, 1)
                split_tile(t, 12)
                if rest:
                    store(t, 2)
                    store(t, 3)
                split_tile(t, 13)
                evacuate1(t, 1)
                split_x(t, 0)
                split_tile(t, 14)
                split_x(t, 1)
                split_tile(t, 15)
                evacuate1(t, 2)
                split_tile(t, 16)
                split_tile(t, 17)
                evacuate1(t, 3)
                if rest:
                    all_stored(t)

            for half in range(2):
                act.wait_ge(raw_landed[half], 16)
                act.activation(in03_hi[:, 4 * half:4 * half + 4, :].rearrange("p k c -> p (k c)"),
                               raw[:, half, :, :].rearrange("p k c -> p (k c)"), ACT.Copy).then_inc(x_hi_ready, 1)
            act.wait_ge(raw_landed[2], 16)
            act.activation(awr_hi[:, :, 0:ER], raw[:, 2, :, :], ACT.Copy).then_inc(awr_hi_ready, 1)
            act.wait_ge(wr_landed, 16)
            act.activation(awr_hi[:, :, ER:HL], wr_raw[:, :, :], ACT.Copy).then_inc(awr_hi_ready, 1)
            act.wait_ge(raw_landed[3], 16)
            act.activation(b0_hi[:, :], raw[:, 3, :, :].rearrange("p k c -> p (k c)"),
                           ACT.Copy).then_inc(b0_hi_ready, 1)
            for q in range(4):
                split_tile(0, q)
            gates(0)
            for q in range(4, OT):
                split_tile(0, q)
            split_gated(0)
            for p in range(PAIRS):
                evacuate0(0, p)
            split_tile(0, OT)
            split_tile(0, OT + 1)
            act.wait_ge(l0_done, OT)
            layer1_phase(0, False)

            with act.Fori(1, BATCHES) as t:
                gates(t)
                split_layer3(t)
                split_gated(t)
                for p in range(PAIRS):
                    evacuate0(t, p)
                for p in range(PAIRS):
                    split_tile(t, 2 * p + 2)
                    split_tile(t, 2 * p + 3)
                    evacuate2(t, p)
                layer1_phase(t, True)

            split_layer3(BATCHES)
            for p in range(PAIRS):
                if p < PAIRS - 1:
                    split_tile(BATCHES, 2 * p + 2, last=True)
                    split_tile(BATCHES, 2 * p + 3, last=True)
                evacuate2(BATCHES, p)
            split_rank(BATCHES)
            for p in range(PAIRS):
                store(BATCHES, p)
            all_stored(BATCHES)

        @block.vector
        def _(dve):
            def finish_raw(t, q):
                j = CHUNKS.index(q % (2 * OT))
                tt = t if q < 2 * OT else t + 1
                i = q % OT
                slot = slot_of(j)
                if OT <= q < 2 * OT:
                    if isinstance(t, int):
                        dve.wait_ge(w1_landed[i], 16)
                        dve.tensor_tensor(w1_full[:, i, i, :], w1_full[:, i, i, :], ident[:, :],
                                          ALU.add).then_inc(w1_diag, 1)
                        dve.wait_ge(w1_diag, i + 1)
                    dve.wait_ge(sign_ready, 8 * t + i + 1)
                    tile = raw[:, slot, :, :].rearrange("p k c -> p (k c)")
                    dve.tensor_tensor(tile, tile, w1_full[:, i, :, :].rearrange("p k c -> p (k c)"),
                                      ALU.add).then_inc(full_ready, 1)
                else:
                    dve.wait_ge(raw_landed[slot], loads_of(tt, j))
                    dve.tensor_tensor(raw[:, slot, i, :], raw[:, slot, i, :], ident[:, :],
                                      ALU.add).then_inc(full_ready, 1)

            def split_tile(t, q, last=False):
                if not last or q + AHEAD < OT:
                    finish_raw(t, q + AHEAD)
                j = CHUNKS.index(q % (2 * OT))
                dve.wait_ge(hi_ready, 16 * t + q + 1)
                if isinstance(t, int) and t == 0 and q < OT:
                    hi, lo = w0_hi[:, q, :, :], w0_lo[:, q, :, :]
                else:
                    hi, lo = hi_ring[:, q % 2, :, :], lo_ring[:, q % 2, :, :]
                    if not (isinstance(t, int) and t == 0 and q < OT + 2):
                        dve.wait_ge(tile_done, 16 * t + q - 9)
                flat = "p k c -> p (k c)"
                dve.tensor_tensor(lo.rearrange(flat), raw[:, slot_of(j), :, :].rearrange(flat),
                                  hi.bitcast(F32).rearrange(flat), ALU.subtract).then_inc(lo_ready, 1)

            def split_x(t, half):
                flat = "p k c -> p (k c)"
                rows = slice(4 * half, 4 * half + 4)
                dve.wait_ge(x_hi_ready, 2 * (t + 1) + half + 1)
                dve.tensor_tensor(in03_lo[:, rows, :].rearrange(flat),
                                  raw[:, slot_of(CHUNKS.index(("x", half))), :, :].rearrange(flat),
                                  in03_hi[:, rows, :].bitcast(F32).rearrange(flat), ALU.subtract
                                  ).then_inc(x_lo_ready, 1)

            def evacuate(sums, hi, lo, done):
                flat = "p k c -> p (k c)"
                dve.tensor_tensor(lo.rearrange(flat), sums, hi.bitcast(F32).rearrange(flat),
                                  ALU.subtract).then_inc(done, 1)

            def evacuate0(t, p):
                dve.wait_ge(in1_hi_ready, 4 * t + p + 1)
                pair = slice(2 * p, 2 * p + 2)
                evacuate(bank[L0_BANK[p]][:, :], in1_hi[:, pair, :], in1_lo[:, pair, :], in1_lo_ready)

            def evacuate1(t, p):
                dve.wait_ge(in2_hi_ready, 8 * t + 2 * p + 2)
                for i in (2 * p, 2 * p + 1):
                    dve.scalar_tensor_tensor(
                        out=in2_lo[:, i, :], in0=bank[L1_BANK[p]][:, (i % 2) * TOKENS:(i % 2 + 1) * TOKENS],
                        scalar=bias_sb[:, i:i + 1], in1=in2_hi[:, i, :].bitcast(F32),
                        op0=ALU.add, op1=ALU.subtract).then_inc(in2_lo_ready, 1)

            def evacuate2(t, p):
                dve.wait_ge(in3_hi_ready, 4 * (t - 1) + p + 1)
                pair = slice(2 * p, 2 * p + 2)
                evacuate(bank[L2_BANK[p]][:, :], in03_hi[:, pair, :], in03_lo[:, pair, :], in3_lo_ready)

            def gates(t):
                steps = [0]

                def step(ins):
                    steps[0] += 1
                    ins.then_inc(gate_step, 1)
                    dve.wait_ge(gate_step, GATE_STEPS * t + steps[0])

                def wide(a):
                    return a.unsqueeze(2).to_broadcast([P, TT, EXPERTS])

                top, top_key, second, second_key, gap, e, g1, g2 = (stat[:, n, :] for n in range(8))
                order = first_key[:, :].unsqueeze(1).to_broadcast([P, TT, EXPERTS])
                dve.wait_ge(down_done, t + 1)
                step(dve.tensor_tensor(logits[:, :, :], down[:, :, ER:HL],
                                       lang_bias[:, bass.ds(t, 1), :].to_broadcast([P, TT, EXPERTS]), ALU.add))
                step(dve.tensor_reduce(top, logits[:, :, :], AX_X, ALU.max))
                step(dve.tensor_tensor(same[:, :, :], logits[:, :, :], wide(top), ALU.is_equal))
                step(dve.tensor_tensor(key[:, :, :], same[:, :, :], order, ALU.mult))
                step(dve.tensor_reduce(top_key, key[:, :, :], AX_X, ALU.max))
                step(dve.tensor_tensor(pick1[:, :, :], key[:, :, :], wide(top_key), ALU.is_equal))
                step(dve.scalar_tensor_tensor(out=rest[:, :, :], in0=pick1[:, :, :], scalar=LOWEST,
                                              in1=logits[:, :, :], op0=ALU.mult, op1=ALU.add))
                step(dve.tensor_reduce(second, rest[:, :, :], AX_X, ALU.max))
                step(dve.tensor_tensor(gap, second, top, ALU.subtract))
                step(dve.tensor_tensor(same[:, :, :], rest[:, :, :], wide(second), ALU.is_equal))
                step(dve.tensor_tensor(key[:, :, :], same[:, :, :], order, ALU.mult))
                step(dve.tensor_reduce(second_key, key[:, :, :], AX_X, ALU.max))
                step(dve.tensor_tensor(pick2[:, :, :], key[:, :, :], wide(second_key), ALU.is_equal))
                dve.wait_ge(exp_ready, t + 1)
                step(dve.tensor_scalar(g1, e, 1.0, None, ALU.add))
                step(dve.reciprocal(g2, g1))
                step(dve.tensor_scalar(g1, g2, SCALING, None, ALU.mult))
                step(dve.tensor_tensor(g2, g1, e, ALU.mult))
                step(dve.tensor_tensor(pick1[:, :, :], pick1[:, :, :], wide(g1), ALU.mult))
                step(dve.tensor_tensor(pick2[:, :, :], pick2[:, :, :], wide(g2), ALU.mult))
                step(dve.tensor_tensor(gates_sb[:, :, :], pick1[:, :, :], pick2[:, :, :], ALU.add))
                assert steps[0] == GATE_STEPS
                shape = [P, TT, EXPERTS, RANK]
                dve.tensor_tensor(gated[:, :, :].rearrange("p s (e r) -> p s e r", r=RANK),
                                  down[:, :, 0:ER].rearrange("p s (e r) -> p s e r", r=RANK),
                                  gates_sb[:, :, :].unsqueeze(3).to_broadcast(shape), ALU.mult
                                  ).then_inc(gated_ready, 1)

            def split_gated(t):
                dve.wait_ge(gatedT_hi_ready, t + 1)
                dve.tensor_tensor(gatedT_lo[:, :], gatedT_ps, gatedT_hi[:, :].bitcast(F32),
                                  ALU.subtract).then_inc(gatedT_lo_ready, 1)

            def take_coeff(t):
                dve.tensor_copy(coeff_now[:, :], coeff_pair[:, bass.ds(t, 1), :].rearrange("p b c -> p (b c)")
                                ).then_inc(coeff_ready, 1)

            def split_layer3(t):
                dve.wait_ge(b3_hi_ready, t)
                for r in range(REP):
                    op = dve.tensor_tensor(b3_split[:, :, r, 1, :], b3_raw[:, :, :],
                                           b3_split[:, :, r, 0, :].bitcast(F32), ALU.subtract)
                op.then_inc(b3_ready, 1)
                dve.wait_ge(a3_hi_ready, t)
                low = slice(4 * RANK, 6 * RANK)
                dve.tensor_tensor(a3_split[low, :], a3_raw[low, :], a3_split[low, :].bitcast(F32),
                                  ALU.subtract).then_inc(a3_ready, 1)

            def split_rank(t):
                dve.wait_ge(rank_hi_ready, t)
                low = slice(2 * RANK, 4 * RANK)
                dve.tensor_tensor(rank_rows[low, :], rank_ps[low, :], rank_rows[low, :].bitcast(F32),
                                  ALU.subtract).then_inc(rank_ready, 1)

            def layer1_phase(t, rest):
                split_tile(t, 10)
                if rest:
                    split_rank(t)
                split_tile(t, 11)
                evacuate1(t, 0)
                split_tile(t, 12)
                split_tile(t, 13)
                evacuate1(t, 1)
                split_x(t, 0)
                split_tile(t, 14)
                split_x(t, 1)
                split_tile(t, 15)
                evacuate1(t, 2)
                split_tile(t, 16)
                split_tile(t, 17)
                evacuate1(t, 3)

            def setup():
                steps = [0]

                def step(ins):
                    steps[0] += 1
                    ins.then_inc(setup_step, 1)
                    dve.wait_ge(setup_step, steps[0])

                dve.wait_ge(small_landed, 48)
                dve.wait_ge(consts_ready, 1)
                step(dve.tensor_copy(expert_no[:, :], expert_i[:, :]))
                step(dve.tensor_scalar(first_key[:, :], expert_no[:, :], -1.0, float(EXPERTS), ALU.mult, ALU.add))
                step(dve.tensor_copy(lang_f[:, :], lang_i[:, :]))
                shape = [P, BATCHES, EXPERTS]
                step(dve.tensor_tensor(lang_bias[:, :, :], lang_f[:, :].unsqueeze(2).to_broadcast(shape),
                                       expert_no[:, :].unsqueeze(1).to_broadcast(shape), ALU.is_equal))
                step(dve.tensor_scalar(lang_bias[:, :, :], lang_bias[:, :, :], LANG_BIAS, None, ALU.mult))
                step(dve.tensor_scalar(coeff_pair[:, :, 0], coeff_all[:, :], 2.0, None, ALU.mult))
                step(dve.tensor_scalar(coeff_pair[:, :, 1], coeff_all[:, :], -1.0, None, ALU.mult))

            flat = "p k c -> p (k c)"
            for half in range(2):
                dve.wait_ge(x_hi_ready, half + 1)
                dve.tensor_tensor(in03_lo[:, 4 * half:4 * half + 4, :].rearrange(flat),
                                  raw[:, half, :, :].rearrange(flat),
                                  in03_hi[:, 4 * half:4 * half + 4, :].bitcast(F32).rearrange(flat),
                                  ALU.subtract).then_inc(x_lo_ready, 1)
            dve.wait_ge(awr_hi_ready, 2)
            dve.tensor_tensor(awr_lo[:, :, ER:HL], wr_raw[:, :, :], awr_hi[:, :, ER:HL].bitcast(F32), ALU.subtract)
            dve.tensor_tensor(awr_lo[:, :, 0:ER], raw[:, 2, :, :], awr_hi[:, :, 0:ER].bitcast(F32),
                              ALU.subtract).then_inc(awr_lo_ready, 1)
            dve.wait_ge(b0_hi_ready, 1)
            dve.tensor_tensor(b0_lo[:, :], raw[:, 3, :, :].rearrange(flat), b0_hi[:, :].bitcast(F32),
                              ALU.subtract).then_inc(b0_lo_ready, 1)
            setup()
            take_coeff(0)
            for q in range(AHEAD):
                finish_raw(0, q)
            for q in range(4):
                split_tile(0, q)
            gates(0)
            for q in range(4, OT):
                split_tile(0, q)
            split_gated(0)
            for p in range(PAIRS):
                evacuate0(0, p)
            split_tile(0, OT)
            split_tile(0, OT + 1)
            layer1_phase(0, False)

            with dve.Fori(1, BATCHES) as t:
                take_coeff(t)
                gates(t)
                split_layer3(t)
                split_gated(t)
                for p in range(PAIRS):
                    evacuate0(t, p)
                for p in range(PAIRS):
                    split_tile(t, 2 * p + 2)
                    split_tile(t, 2 * p + 3)
                    evacuate2(t, p)
                layer1_phase(t, True)

            split_layer3(BATCHES)
            for p in range(PAIRS):
                if p < PAIRS - 1:
                    split_tile(BATCHES, 2 * p + 2, last=True)
                    split_tile(BATCHES, 2 * p + 3, last=True)
                evacuate2(BATCHES, p)
            split_rank(BATCHES)


_OUT = (BATCHES, PAIRS, P, 2 * TOKENS)


def kernel(x, itok_B_0_7, condB_coeff, itok_B_3_7, mask_Bx4096x4096_ik1, L0_cond_W, L0_cond_Wr, L0_cond_A,
           L0_cond_B, L1_cond_W, L1_cond_b, L2_cond_weight, L3_cond_A, L3_cond_B):
    import numpy as np
    import concourse.bacc as bacc
    from concourse.bass_utils import run_bass_kernel_spmd

    def tiles(w):
        lead = w.shape[:-2]
        w = w.reshape(*lead, KT, P, OT, P)
        n = len(lead)
        w = w.transpose(*range(n), n + 2, n + 1, n, n + 3)
        return np.ascontiguousarray(w).reshape(*lead, OT, P, KT * P)

    def inputs_first(w, cols):
        return np.ascontiguousarray(w.reshape(KT, P, cols).transpose(1, 0, 2)).reshape(P, KT * cols)

    a = {k: np.asarray(v) for k, v in dict(
        x=x, lang=itok_B_0_7, coeff=condB_coeff, ids=itok_B_3_7, mask=mask_Bx4096x4096_ik1, w0=L0_cond_W,
        wr=L0_cond_Wr, a0=L0_cond_A, b0=L0_cond_B, w1=L1_cond_W, bias1=L1_cond_b, w2=L2_cond_weight,
        a3=L3_cond_A, b3=L3_cond_B).items()}
    arrays = {
        "x": np.ascontiguousarray(a["x"].reshape(BATCHES, TOKENS, 2, KT // 2, P).transpose(0, 2, 4, 3, 1)
                                  ).reshape(BATCHES, 2, P, KT // 2 * TOKENS),
        "lang_ids": a["lang"],
        "coeff": a["coeff"],
        "ids": a["ids"],
        "mask": tiles(a["mask"]),
        "w0": tiles(a["w0"].T),
        "wr": inputs_first(a["wr"].T, EXPERTS),
        "a0": inputs_first(a["a0"].reshape(ER, D).T, ER),
        "b0": np.ascontiguousarray(a["b0"].transpose(0, 2, 1)).reshape(ER, D),
        "w1": tiles(a["w1"].T),
        "bias1": np.ascontiguousarray(a["bias1"].reshape(OT, P).T),
        "w2": tiles(a["w2"].transpose(0, 2, 1)),
        "a3": np.ascontiguousarray(a["a3"].transpose(0, 2, 1)),
        "b3": np.ascontiguousarray(a["b3"].reshape(EXPERTS, RANK, KT, P).transpose(0, 3, 2, 1)
                                   ).reshape(EXPERTS, P, KT * RANK),
    }
    nc = bacc.Bacc("TRN2", target_bir_lowering=False, num_devices=1, dynamic_dma_scratch_size=1024)
    args = [nc.dram_tensor(f"in_{name}", v.shape, mybir.dt.from_np(v.dtype), kind="ExternalInput").ap()
            for name, v in arrays.items()]
    out = nc.dram_tensor("out_0", _OUT, F32, kind="ExternalOutput").ap()
    cond_resid_kernel(nc, *args, out)
    got = run_bass_kernel_spmd(nc, [{f"in_{n}": v for n, v in arrays.items()}], core_ids=[0])
    y = got.results[0]["out_0"].reshape(BATCHES, PAIRS, P, 2, TOKENS)
    return np.ascontiguousarray(y.transpose(0, 4, 1, 3, 2)).reshape(BATCHES, TOKENS, D)
```

```python
from contextlib import ExitStack

import concourse.bass as bass
from concourse import mybir

P = 128
BATCHES = 8
TOKENS = 256
D = 1024
KT = D // P
OT = D // P
PAIRS = OT // 2
TT = TOKENS // P
EXPERTS = 8
RANK = 16
ER = EXPERTS * RANK
HL = ER + EXPERTS
LANG_BIAS = 5.0
SCALING = 2.0
LOWEST = -3.0e38
RING = 6
AHEAD = 1
PER_ITER = 18
REP = 3
ROWS3 = REP * 2 * RANK

F32 = mybir.dt.float32
F32R = mybir.dt.float32r
I32 = mybir.dt.int32
ALU = mybir.AluOpType
ACT = mybir.ActivationFunctionType
AX_X = mybir.AxisListType.X

CHUNKS = list(range(11)) + [("x", 0), 11, ("x", 1)] + list(range(12, 16))
X_HALVES = [("x", 0), ("x", 1)]
L0_BANK = [0, 1, 6, 7]
L1_BANK = [6, 7, 6, 7]
L2_BANK = [2, 3, 0, 1]
STORE_ORDER = [2, 3, 0, 1]
GATE_STEPS = 22
WARM_UP = 24


def cond_resid_kernel(nc, x, lang_ids, coeff, ids, mask, w0, wr, a0, b0, w1, bias1, w2, a3, b3, out):
    ctx = ExitStack()
    with ctx:
        def sb(name, shape, dt=F32):
            return ctx.enter_context(nc.sbuf_tensor(name, shape, dt))

        def sem(name):
            return ctx.enter_context(nc.semaphore(name))

        w0_hi = sb("w0_hi", [P, OT, KT, P], F32R)
        w0_lo = sb("w0_lo", [P, OT, KT, P], F32R)
        w1_full = sb("w1_full", [P, OT, KT, P])
        x0_raw = [w1_full[:, OT - 4 + half, :, :].rearrange("p k c -> p (k c)") for half in range(2)]
        a0_raw, b0_raw = w1_full[:, OT - 2, :, :], w1_full[:, OT - 1, :, :].rearrange("p k c -> p (k c)")
        awr = sb("awr", [P, KT, 2, HL], F32R)
        b0_hi = sb("b0_hi", [P, D], F32R)
        b0_lo = sb("b0_lo", [P, D], F32R)
        raw = sb("raw", [P, RING, KT, P])
        hi_ring = sb("hi_ring", [P, 2, KT, P], F32R)
        lo_ring = sb("lo_ring", [P, 2, KT, P], F32R)
        in03_hi = sb("in03_hi", [P, KT, TOKENS], F32R)
        in03_lo = sb("in03_lo", [P, KT, TOKENS], F32R)
        in1_hi = sb("in1_hi", [P, KT, TOKENS], F32R)
        in1_lo = sb("in1_lo", [P, KT, TOKENS], F32R)
        in2_hi = sb("in2_hi", [P, KT, TOKENS], F32R)
        in2_lo = sb("in2_lo", [P, KT, TOKENS], F32R)
        gated = sb("gated", [P, TT, ER])
        gatedT_hi = sb("gatedT_hi", [P, TOKENS], F32R)
        gatedT_lo = sb("gatedT_lo", [P, TOKENS], F32R)
        logits = sb("logits", [P, TT, EXPERTS])
        rest = sb("rest", [P, TT, EXPERTS])
        same = sb("same", [P, TT, EXPERTS])
        key = sb("key", [P, TT, EXPERTS])
        pick1 = sb("pick1", [P, TT, EXPERTS])
        pick2 = sb("pick2", [P, TT, EXPERTS])
        gates = sb("gates", [P, TT, EXPERTS])
        stat = sb("stat", [P, 8, TT])
        a3_raw = sb("a3_raw", [ROWS3, D])
        a3_split = sb("a3_split", [ROWS3, D], F32R)
        b3_raw = sb("b3_raw", [P, KT, RANK])
        b3_split = sb("b3_split", [P, KT, REP, 2, RANK], F32R)
        rank_rows = sb("rank_rows", [ROWS3, TOKENS], F32R)
        stage = sb("stage", [P, 2, 2 * TOKENS])
        ident = sb("ident", [P, P])
        first_key = sb("first_key", [P, EXPERTS])
        expert_no = sb("expert_no", [P, EXPERTS])
        expert_i = sb("expert_i", [P, EXPERTS], I32)
        lang_i = sb("lang_i", [P, BATCHES], I32)
        lang_f = sb("lang_f", [P, BATCHES])
        lang_bias = sb("lang_bias", [P, BATCHES, EXPERTS])
        ids_row = sb("ids_row", [1, BATCHES], I32)
        coeff_all = sb("coeff_all", [P, BATCHES])
        coeff_pair = sb("coeff_pair", [P, BATCHES, 2])
        coeff_now = sb("coeff_now", [P, 2])
        wr_raw = sb("wr_raw", [P, KT, EXPERTS])
        bias_sb = sb("bias_sb", [P, OT])
        sums = ctx.enter_context(nc.psum_tensor("sums", [P, 8, 2 * TOKENS], F32))
        bank = [sums[:, i, :] for i in range(8)]
        down_hi = sums[:, 4:4 + TT, 0:HL]
        down_lo = sums[:, 4:4 + TT, HL:2 * HL]
        gatedT_ps = bank[5][:, 0:TOKENS]
        rank_ps = bank[5][0:ROWS3, TOKENS:2 * TOKENS]

        x_landed = [sem("x_landed0"), sem("x_landed1")]
        a0_landed, b0_landed = sem("a0_landed"), sem("b0_landed")
        raw_landed = [sem(f"raw_landed{s}") for s in range(RING)]
        w1_landed = [sem(f"w1_landed{i}") for i in range(OT)]
        wr_landed = sem("wr_landed")
        small_landed, ids_landed = sem("small_landed"), sem("ids_landed")
        a3_landed, b3_landed = sem("a3_landed"), sem("b3_landed")
        out_stored = [sem("out_stored0"), sem("out_stored1")]
        last_staged, last_stored = sem("last_staged"), sem("last_stored")
        zeroed, consts_ready, setup_step = sem("zeroed"), sem("consts_ready"), sem("setup_step")
        awr_hi_ready, awr_lo_ready = sem("awr_hi_ready"), sem("awr_lo_ready")
        b0_hi_ready, b0_lo_ready = sem("b0_hi_ready"), sem("b0_lo_ready")
        w1_diag, coeff_ready = sem("w1_diag"), sem("coeff_ready")
        sign_ready, full_ready, w0_full = sem("sign_ready"), sem("full_ready"), sem("w0_full")
        hi_ready, lo_ready = sem("hi_ready"), sem("lo_ready")
        hi_used, tile_done = sem("hi_used"), sem("tile_done")
        x_hi_ready, x_lo_ready = sem("x_hi_ready"), sem("x_lo_ready")
        down_lo_copied = sem("down_lo_copied")
        down_done, gate_step, exp_ready = sem("down_done"), sem("gate_step"), sem("exp_ready")
        gated_ready, gatedT_done = sem("gated_ready"), sem("gatedT_done")
        gatedT_hi_ready, gatedT_lo_ready = sem("gatedT_hi_ready"), sem("gatedT_lo_ready")
        l0_done = sem("l0_done")
        in1_hi_ready, in1_lo_ready = sem("in1_hi_ready"), sem("in1_lo_ready")
        in2_hi_ready, in2_lo_ready = sem("in2_hi_ready"), sem("in2_lo_ready")
        in3_hi_ready, in3_lo_ready = sem("in3_hi_ready"), sem("in3_lo_ready")
        a3_hi_ready, a3_ready = sem("a3_hi_ready"), sem("a3_ready")
        b3_hi_ready, b3_ready = sem("b3_hi_ready"), sem("b3_ready")
        rank_done, rank_hi_ready, rank_ready = sem("rank_done"), sem("rank_hi_ready"), sem("rank_ready")
        l3_done, staged = sem("l3_done"), sem("staged")

        block = ctx.enter_context(nc.Block())

        def slot_of(j):
            return j % RING

        def is_loaded(t, j):
            return not (isinstance(t, int) and t == BATCHES - 1 and CHUNKS[j] in X_HALVES)

        def loads_of(t, j):
            n = t * (PER_ITER // RING) + j // RING + 1
            if isinstance(t, int) and t >= BATCHES - 1:
                n -= sum(slot_of(h) == slot_of(j) and not is_loaded(BATCHES - 1, h)
                         for h in range(j if t == BATCHES - 1 else PER_ITER))
            return 16 * n

        @block.sync
        def _(sp):
            def free_slot(t, j):
                j -= RING
                tt = t if j >= 0 else t - 1
                if not is_loaded(tt, j % PER_ITER):
                    j -= RING
                    assert j >= 0 or tt == t - 1
                before = CHUNKS[j % PER_ITER]
                if before in X_HALVES:
                    sp.wait_ge(x_lo_ready, 2 * (tt + 1) + before[1] + 1)
                else:
                    sp.wait_ge(lo_ready, 16 * tt + before + 1)

            def load_raw(slot, src, dtype=F32):
                dst = raw[:, slot, :, :].rearrange("p k c -> p (k c)")
                sp.dma_start(dst if dtype == F32 else dst.bitcast(dtype), src).then_inc(raw_landed[slot], 16)

            def load_x(batch, half, slot):
                load_raw(slot, x[bass.ds(batch, 1), half, :, :].rearrange("b p c -> (b p) c"))

            def load_chunk(t, j, expert):
                c, slot = CHUNKS[j], slot_of(j)
                if c in X_HALVES:
                    load_x(t + 1, c[1], slot)
                elif c >= OT:
                    load_raw(slot, mask[bass.ds(t, 1), c - OT, :, :].rearrange("b p c -> (b p) c"), I32)
                elif expert is None:
                    load_raw(slot, w0[c])
                else:
                    load_raw(slot, w2[bass.ds(expert, 1), c, :, :].rearrange("e p c -> (e p) c"))

            def id_of(t):
                return sp.value_load(ids_row[0:1, bass.ds(t, 1)], min_val=0, max_val=EXPERTS - 1)

            def load_layer3(t):
                expert = id_of(t)
                for r in range(2 * REP):
                    sp.dma_start(a3_raw[RANK * r:RANK * (r + 1), :],
                                 a3[bass.ds(expert, 1), :, :].rearrange("e r o -> (e r) o")
                                 ).then_inc(a3_landed, 16)
                sp.dma_start(b3_raw[:, :, :].rearrange("p k r -> p (k r)"),
                             b3[bass.ds(expert, 1), :, :].rearrange("e p c -> (e p) c")
                             ).then_inc(b3_landed, 16)

            def load_flat(dst, src, landed):
                sp.dma_start(dst, src).then_inc(landed, 16)

            load_chunk(0, 0, None)
            for half in range(2):
                load_flat(x0_raw[half], x[0, half], x_landed[half])
            load_chunk(0, 1, None)
            load_flat(a0_raw.rearrange("p k c -> p (k c)"), a0, a0_landed)
            load_flat(wr_raw[:, :, :].rearrange("p k e -> p (k e)"), wr, wr_landed)
            load_flat(lang_i[:, :], lang_ids.partition_broadcast(P), small_landed)
            load_flat(coeff_all[:, :], coeff.partition_broadcast(P), small_landed)
            load_flat(bias_sb[:, :], bias1, small_landed)
            load_flat(ids_row[:, :], ids.partition_broadcast(1), ids_landed)
            for j in range(2, PER_ITER):
                if j == 4:
                    load_flat(b0_raw, b0, b0_landed)
                if j >= RING:
                    free_slot(0, j)
                load_chunk(0, j, None)
                if CHUNKS[j] in range(OT - 2, 2 * OT - 2):
                    i = CHUNKS[j] - (OT - 2)
                    if i in (OT - 4, OT - 3):
                        sp.wait_ge(x_lo_ready, i - (OT - 4) + 1)
                    elif i == OT - 2:
                        sp.wait_ge(awr_lo_ready, 1)
                    elif i == OT - 1:
                        sp.wait_ge(b0_lo_ready, 1)
                    sp.dma_start(w1_full[:, i, :, :].rearrange("p k c -> p (k c)"), w1[i]
                                 ).then_inc(w1_landed[i], 16)
            sp.wait_ge(ids_landed, 16)
            load_layer3(0)

            def iteration(t):
                expert = id_of(t - 1)
                for j in range(PER_ITER):
                    if is_loaded(t, j):
                        free_slot(t, j)
                        load_chunk(t, j, expert)
                sp.wait_ge(a3_ready, t)
                sp.wait_ge(b3_ready, t)
                load_layer3(t)

            with sp.Fori(1, BATCHES - 1) as t:
                iteration(t)
            iteration(BATCHES - 1)

            expert = id_of(BATCHES - 1)
            for j in range(OT):
                free_slot(BATCHES, j)
                load_chunk(BATCHES, j, expert)
            for n, p in enumerate((1, 3)):
                sp.wait_ge(last_staged, n + 1)
                sp.dma_start(out[BATCHES - 1, p], raw[:, p, 0:4, :].rearrange("p k c -> p (k c)")
                             ).then_inc(last_stored, 16)
            sp.wait_ge(last_stored, 64)

        @block.gpsimd
        def _(pool):
            pool.iota(expert_i[:, :], [[1, EXPERTS]], base=0, channel_multiplier=0).then_inc(zeroed, 1)
            pool.memset(ident[:, :], 0.0).then_inc(zeroed, 1)
            pool.wait_ge(zeroed, 2)
            pool.affine_select(out=ident[:, :], in_=ident[:, :], compare_op=ALU.not_equal, fill=1.0,
                               base=0, pattern=[[-1, P]], channel_multiplier=1).then_inc(consts_ready, 1)
            pool.wait_ge(consts_ready, 1)
            for q in range(OT):
                block = raw[:, slot_of(q), q, :]
                pool.wait_ge(raw_landed[slot_of(q)], loads_of(0, q))
                pool.tensor_tensor(block, block, ident[:, :], ALU.add).then_inc(w0_full, 1)

        @block.tensor
        def _(pe):
            def product(o, parts, first, last, done=None):
                for n, (w, v) in enumerate(parts):
                    mm = pe.matmul(o, w, v, start=first and n == 0, stop=last and n == len(parts) - 1,
                                   skip_group_check=True)
                if done is not None:
                    mm.then_inc(done, 1)

            def half_of(b, i):
                return bank[b][:, (i % 2) * TOKENS:(i % 2 + 1) * TOKENS]

            def down_projections(t):
                for half in range(2):
                    pe.wait_ge(x_lo_ready, 2 * t + half + 1)
                    for s in range(TT):
                        tok = slice(s * P, (s + 1) * P)
                        for k in range(4 * half, 4 * half + 4):
                            product(bank[4 + s][:, 0:2 * HL],
                                    [(in03_hi[:, k, tok], awr[:, k, :, :].rearrange("p a c -> p (a c)"))],
                                    k == 0, k == KT - 1)
                            product(bank[4 + s][:, 0:HL], [(in03_lo[:, k, tok], awr[:, k, 0, :])],
                                    False, k == KT - 1, down_done if s == TT - 1 and k == KT - 1 else None)

            def base0(t, i):
                in_batch0 = isinstance(t, int) and t == 0
                if in_batch0:
                    pe.wait_ge(hi_ready, i + 1)
                o = half_of(L0_BANK[i // 2], i)
                parts = []
                for k in range(KT):
                    parts += [(w0_hi[:, i, k, :], in03_hi[:, k, :]), (w0_hi[:, i, k, :], in03_lo[:, k, :])]
                product(o, parts, i % 2 == 0, False)
                if in_batch0:
                    pe.wait_ge(lo_ready, i + 1)
                product(o, [(w0_lo[:, i, k, :], in03_hi[:, k, :]) for k in range(KT)], False, False)

            def warm_up():
                pe.wait_ge(consts_ready, 1)
                for _ in range(WARM_UP):
                    pe.transpose(gatedT_ps[:, 0:P], ident[:, :], ident[:, :])

            def first_base0():
                o = half_of(L0_BANK[0], 0)
                for half in range(2):
                    rows = range(4 * half, 4 * half + 4)
                    pe.wait_ge(hi_ready, 1)
                    pe.wait_ge(x_hi_ready, half + 1)
                    product(o, [(w0_hi[:, 0, k, :], in03_hi[:, k, :]) for k in rows], half == 0, False)
                    pe.wait_ge(lo_ready, 1)
                    product(o, [(w0_lo[:, 0, k, :], in03_hi[:, k, :]) for k in rows], False, False)
                    pe.wait_ge(x_lo_ready, half + 1)
                    product(o, [(w0_hi[:, 0, k, :], in03_lo[:, k, :]) for k in rows], False, False)

            def turn_gated(t):
                pe.wait_ge(gated_ready, t + 1)
                for s in range(TT):
                    mm = pe.transpose(gatedT_ps[:, s * P:(s + 1) * P], gated[:, s, :], ident[:, :])
                mm.then_inc(gatedT_done, 1)

            def up0(t, i):
                cols = slice(i * P, (i + 1) * P)
                product(half_of(L0_BANK[i // 2], i),
                        [(b0_hi[:, cols], gatedT_hi[:, :]), (b0_hi[:, cols], gatedT_lo[:, :]),
                         (b0_lo[:, cols], gatedT_hi[:, :])], False, True, l0_done)

            def streamed(t, q, banks, in_hi, in_lo, in_ready):
                i, slot = q % OT, q % 2
                o = half_of(banks[i // 2], i)
                pe.wait_ge(hi_ready, 16 * t + q + 1)
                early = range(KT - 2) if i == 0 else range(KT)
                for k in early:
                    if i == 0:
                        in_ready(k)
                    product(o, [(hi_ring[:, slot, k, :], in_hi[:, k, :]), (hi_ring[:, slot, k, :], in_lo[:, k, :])],
                            i % 2 == 0 and k == 0, False, hi_used if k == KT - 1 else None)
                pe.wait_ge(lo_ready, 16 * t + q + 1)
                product(o, [(lo_ring[:, slot, k, :], in_hi[:, k, :]) for k in early], False, i > 0,
                        tile_done if i > 0 else None)
                if i == 0:
                    for k in range(KT - 2, KT):
                        in_ready(k)
                        product(o, [(hi_ring[:, slot, k, :], in_hi[:, k, :]), (hi_ring[:, slot, k, :], in_lo[:, k, :])],
                                False, False, hi_used if k == KT - 1 else None)
                    product(o, [(lo_ring[:, slot, k, :], in_hi[:, k, :]) for k in range(KT - 2, KT)], False, True,
                            tile_done)

            def layer1(t, i):
                def in_ready(k):
                    if k % 2 == 0 and k >= 4:
                        pe.wait_ge(in1_lo_ready, 4 * t + k // 2 + 1)
                if i == 0:
                    pe.wait_ge(in1_lo_ready, 4 * t + 3)
                if i in (4, 6):
                    pe.wait_ge(in2_lo_ready, 8 * t + i - 2)
                streamed(t, OT + i, L1_BANK, in1_hi, in1_lo, in_ready)

            def layer2(t, i):
                streamed(t, i, L2_BANK, in2_hi, in2_lo,
                         lambda k: pe.wait_ge(in2_lo_ready, 8 * (t - 1) + k + 1))

            def layer3_rank(t):
                pe.wait_ge(b3_ready, t)
                for k in range(KT):
                    if k % 2 == 0:
                        pe.wait_ge(in3_lo_ready, 4 * (t - 1) + k // 2 + 1)
                    w = b3_split[:, k, :, :, :].rearrange("p a b c -> p (a b c)")
                    product(rank_ps, [(w, in03_hi[:, k, :]), (w, in03_lo[:, k, :])],
                            k == 0, k == KT - 1, rank_done if k == KT - 1 else None)

            def layer3_up(t):
                pe.wait_ge(a3_ready, t)
                pe.wait_ge(rank_ready, t)
                for i in range(OT):
                    product(half_of(L2_BANK[i // 2], i),
                            [(a3_split[:, i * P:(i + 1) * P], rank_rows[:, :])],
                            False, True, l3_done if i % 2 else None)

            def layer1_phase(t, before, after):
                layer1(t, 0)
                if before:
                    layer3_rank(t)
                layer1(t, 1)
                if before:
                    layer3_up(t)
                layer1(t, 2)
                layer1(t, 3)
                if after:
                    down_projections(t + 1)
                layer1(t, 4)
                if after:
                    base0(t + 1, 0)
                layer1(t, 5)
                if after:
                    base0(t + 1, 1)
                layer1(t, 6)
                if after:
                    base0(t + 1, 2)
                    turn_gated(t + 1)
                layer1(t, 7)
                if after:
                    pe.wait_ge(gatedT_lo_ready, t + 2)
                    up0(t + 1, 0)
                    up0(t + 1, 1)
                    base0(t + 1, 3)
                    up0(t + 1, 2)
                    up0(t + 1, 3)

            def layer2_phase(t):
                for i in range(4):
                    layer2(t, i)
                    base0(t, 4 + i)
                    up0(t, 4 + i)
                for i in range(4, OT):
                    layer2(t, i)

            warm_up()
            first_base0()
            base0(0, 1)
            pe.wait_ge(awr_lo_ready, 1)
            down_projections(0)
            for i in range(2, 5):
                base0(0, i)
            turn_gated(0)
            base0(0, 5)
            pe.wait_ge(b0_lo_ready, 1)
            pe.wait_ge(gatedT_lo_ready, 1)
            for i in range(6):
                up0(0, i)
            for i in range(6, OT):
                base0(0, i)
                up0(0, i)
            layer1_phase(0, False, True)

            with pe.Fori(1, BATCHES - 1) as t:
                layer2_phase(t)
                layer1_phase(t, True, True)
            layer2_phase(BATCHES - 1)
            layer1_phase(BATCHES - 1, True, False)

            for i in range(OT):
                layer2(BATCHES, i)
            layer3_rank(BATCHES)
            layer3_up(BATCHES)

        @block.scalar
        def _(act):
            def finish_raw(t, q):
                if not OT <= q < 2 * OT:
                    return
                j = CHUNKS.index(q)
                tile = raw[:, slot_of(j), :, :].rearrange("p k c -> p (k c)")
                if q == OT:
                    act.wait_ge(coeff_ready, t + 1)
                act.wait_ge(raw_landed[slot_of(j)], loads_of(t, j))
                act.activation(tile, tile.bitcast(I32), ACT.Identity, bias=coeff_now[:, 1:2],
                               scale=coeff_now[:, 0:1]).then_inc(sign_ready, 1)

            def split_tile(t, q, last=False):
                if not last:
                    finish_raw(t, q + AHEAD)
                split_high(t, q)

            def split_high(t, q):
                j = CHUNKS.index(q % (2 * OT))
                if isinstance(t, int) and t == 0 and q < OT:
                    act.wait_ge(w0_full, q + 1)
                    dst = w0_hi[:, q, :, :]
                else:
                    act.wait_ge(full_ready, 16 * t + q - 7)
                    dst = hi_ring[:, q % 2, :, :]
                    if not (isinstance(t, int) and t == 0 and q < OT + 2):
                        act.wait_ge(hi_used, 16 * t + q - 9)
                        act.wait_ge(lo_ready, 16 * t + q - 1)
                act.activation(dst, raw[:, slot_of(j), :, :], ACT.Copy).then_inc(hi_ready, 1)

            def split_x(t, half):
                j = CHUNKS.index(("x", half))
                act.wait_ge(raw_landed[slot_of(j)], loads_of(t, j))
                act.activation(in03_hi[:, 4 * half:4 * half + 4, :].rearrange("p k c -> p (k c)"),
                               raw[:, slot_of(j), :, :].rearrange("p k c -> p (k c)"),
                               ACT.Copy).then_inc(x_hi_ready, 1)

            def evacuate0(t, p):
                act.wait_ge(l0_done, 8 * t + 2 * p + 2)
                act.activation(in1_hi[:, 2 * p:2 * p + 2, :].rearrange("p k c -> p (k c)"),
                               bank[L0_BANK[p]][:, :], ACT.Copy).then_inc(in1_hi_ready, 1)

            def evacuate1(t, p):
                act.wait_ge(tile_done, 16 * t + 2 * p + 2)
                for i in (2 * p, 2 * p + 1):
                    act.activation(in2_hi[:, i, :], bank[L1_BANK[p]][:, (i % 2) * TOKENS:(i % 2 + 1) * TOKENS],
                                   ACT.Identity, bias=bias_sb[:, i:i + 1]).then_inc(in2_hi_ready, 1)

            def evacuate2(t, p):
                act.wait_ge(tile_done, 16 * t + 2 * p - 6)
                act.activation(in03_hi[:, 2 * p:2 * p + 2, :].rearrange("p k c -> p (k c)"),
                               bank[L2_BANK[p]][:, :], ACT.Copy).then_inc(in3_hi_ready, 1)

            def gap_exp(t):
                act.wait_ge(gate_step, GATE_STEPS * t + 2)
                act.activation(gated[:, :, :], down_lo[:, :, 0:ER], ACT.Copy).then_inc(down_lo_copied, 1)
                act.wait_ge(gate_step, GATE_STEPS * t + 10)
                act.activation(stat[:, 5, :], stat[:, 4, :], ACT.Exp).then_inc(exp_ready, 1)

            def split_gated(t):
                act.wait_ge(gatedT_done, t + 1)
                act.activation(gatedT_hi[:, :], gatedT_ps, ACT.Copy).then_inc(gatedT_hi_ready, 1)

            def split_layer3(t):
                act.wait_ge(b3_landed, 16 * t)
                for r in range(REP):
                    op = act.activation(b3_split[:, :, r, 0, :], b3_raw[:, :, :], ACT.Copy)
                op.then_inc(b3_hi_ready, 1)
                act.wait_ge(a3_landed, 16 * 2 * REP * t)
                act.activation(a3_split[:, :], a3_raw[:, :], ACT.Copy).then_inc(a3_hi_ready, 1)

            def split_rank(t):
                act.wait_ge(rank_done, t)
                act.activation(rank_rows[:, :], rank_ps, ACT.Copy).then_inc(rank_hi_ready, 1)

            def store(t, p):
                n = STORE_ORDER.index(p)
                if n >= 2:
                    act.wait_ge(out_stored[p % 2], 16 * (2 * (t - 1) + 1))
                act.wait_ge(l3_done, 4 * (t - 1) + p + 1)
                act.activation(stage[:, p % 2, :], bank[L2_BANK[p]][:, :], ACT.Copy).then_inc(staged, 1)
                act.wait_ge(staged, 4 * (t - 1) + n + 1)
                act.dma_start(out[bass.ds(t - 1, 1), p, :, :].rearrange("b p c -> (b p) c"),
                              stage[:, p % 2, :]).then_inc(out_stored[p % 2], 16)

            def all_stored(t):
                for s in range(2):
                    act.wait_ge(out_stored[s], 16 * 2 * t)

            def layer1_phase(t, before, after):
                split_tile(t, 10)
                if before:
                    split_rank(t)
                split_tile(t, 11)
                if after:
                    split_x(t, 0)
                    split_x(t, 1)
                evacuate1(t, 0)
                if before:
                    store(t, 2)
                    store(t, 3)
                split_tile(t, 12)
                if before and after:
                    store(t, 0)
                    store(t, 1)
                split_tile(t, 13)
                evacuate1(t, 1)
                if after:
                    gap_exp(t + 1)
                split_tile(t, 14)
                if not after:
                    store(t, 0)
                split_tile(t, 15)
                if not after:
                    store(t, 1)
                evacuate1(t, 2)
                split_tile(t, 16)
                if after:
                    split_gated(t + 1)
                evacuate1(t, 3)
                split_tile(t, 17)
                if after:
                    evacuate0(t + 1, 0)
                    evacuate0(t + 1, 1)
                if before:
                    all_stored(t)

            def layer2_phase(t):
                split_layer3(t)
                split_tile(t, 2)
                split_tile(t, 3)
                evacuate0(t, 2)
                split_tile(t, 4)
                split_tile(t, 5)
                evacuate0(t, 3)
                evacuate2(t, 0)
                evacuate2(t, 1)
                split_tile(t, 6)
                split_tile(t, 7)
                evacuate2(t, 2)
                split_tile(t, 8)
                split_tile(t, 9)
                evacuate2(t, 3)

            split_tile(0, 0)
            for half in range(2):
                rows = slice(4 * half, 4 * half + 4)
                act.wait_ge(x_landed[half], 16)
                act.activation(in03_hi[:, rows, :].rearrange("p k c -> p (k c)"), x0_raw[half], ACT.Copy).then_inc(x_hi_ready, 1)
            split_tile(0, 1)
            act.wait_ge(a0_landed, 16)
            act.activation(awr[:, :, 0, 0:ER], a0_raw,
                           ACT.Copy).then_inc(awr_hi_ready, 1)
            act.wait_ge(wr_landed, 16)
            act.activation(awr[:, :, 0, ER:HL], wr_raw[:, :, :], ACT.Copy).then_inc(awr_hi_ready, 1)
            split_tile(0, 2)
            split_tile(0, 3)
            act.wait_ge(b0_landed, 16)
            act.activation(b0_hi[:, :], b0_raw, ACT.Copy).then_inc(b0_hi_ready, 1)
            split_tile(0, 4)
            gap_exp(0)
            split_tile(0, 5)
            split_gated(0)
            split_tile(0, 6)
            split_tile(0, 7)
            evacuate0(0, 0)
            evacuate0(0, 1)
            split_tile(0, 8)
            evacuate0(0, 2)
            split_high(0, 9)
            evacuate0(0, 3)
            finish_raw(0, 10)
            layer1_phase(0, False, True)

            with act.Fori(1, BATCHES - 1) as t:
                layer2_phase(t)
                layer1_phase(t, True, True)
            layer2_phase(BATCHES - 1)
            layer1_phase(BATCHES - 1, True, False)

            split_layer3(BATCHES)
            for p in range(PAIRS):
                if p < PAIRS - 1:
                    split_tile(BATCHES, 2 * p + 2, last=True)
                    split_tile(BATCHES, 2 * p + 3, last=True)
                evacuate2(BATCHES, p)
            split_rank(BATCHES)
            for p in (0, 2):
                act.wait_ge(l3_done, 4 * (BATCHES - 1) + p + 1)
                act.activation(stage[:, p // 2, :], bank[L2_BANK[p]][:, :], ACT.Copy).then_inc(staged, 1)
                act.wait_ge(staged, 4 * (BATCHES - 1) + p // 2 + 1)
                act.dma_start(out[BATCHES - 1, p], stage[:, p // 2, :]).then_inc(last_stored, 16)
            act.wait_ge(last_stored, 64)

        @block.vector
        def _(dve):
            def finish_raw(t, q):
                if isinstance(t, int) and t == 0 and q < OT:
                    return
                j = CHUNKS.index(q % (2 * OT))
                tt = t if q < 2 * OT else t + 1
                i = q % OT
                slot = slot_of(j)
                if OT <= q < 2 * OT:
                    if isinstance(t, int) and t == 0:
                        dve.wait_ge(w1_landed[i], 16)
                        dve.tensor_tensor(w1_full[:, i, i, :], w1_full[:, i, i, :], ident[:, :],
                                          ALU.add).then_inc(w1_diag, 1)
                        dve.wait_ge(w1_diag, i + 1)
                    dve.wait_ge(sign_ready, 8 * t + i + 1)
                    tile = raw[:, slot, :, :].rearrange("p k c -> p (k c)")
                    dve.tensor_tensor(tile, tile, w1_full[:, i, :, :].rearrange("p k c -> p (k c)"),
                                      ALU.add).then_inc(full_ready, 1)
                else:
                    dve.wait_ge(raw_landed[slot], loads_of(tt, j))
                    dve.tensor_tensor(raw[:, slot, i, :], raw[:, slot, i, :], ident[:, :],
                                      ALU.add).then_inc(full_ready, 1)

            def split_tile(t, q, last=False):
                if not last or q + AHEAD < OT:
                    finish_raw(t, q + AHEAD)
                split_low(t, q)

            def split_low(t, q):
                j = CHUNKS.index(q % (2 * OT))
                dve.wait_ge(hi_ready, 16 * t + q + 1)
                if isinstance(t, int) and t == 0 and q < OT:
                    hi, lo = w0_hi[:, q, :, :], w0_lo[:, q, :, :]
                else:
                    hi, lo = hi_ring[:, q % 2, :, :], lo_ring[:, q % 2, :, :]
                    if not (isinstance(t, int) and t == 0 and q < OT + 2):
                        dve.wait_ge(tile_done, 16 * t + q - 9)
                flat = "p k c -> p (k c)"
                dve.tensor_tensor(lo.rearrange(flat), raw[:, slot_of(j), :, :].rearrange(flat),
                                  hi.bitcast(F32).rearrange(flat), ALU.subtract).then_inc(lo_ready, 1)

            def split_x(t, half):
                flat = "p k c -> p (k c)"
                rows = slice(4 * half, 4 * half + 4)
                dve.wait_ge(x_hi_ready, 2 * (t + 1) + half + 1)
                dve.tensor_tensor(in03_lo[:, rows, :].rearrange(flat),
                                  raw[:, slot_of(CHUNKS.index(("x", half))), :, :].rearrange(flat),
                                  in03_hi[:, rows, :].bitcast(F32).rearrange(flat), ALU.subtract
                                  ).then_inc(x_lo_ready, 1)

            def evacuate(sums, hi, lo, done):
                flat = "p k c -> p (k c)"
                dve.tensor_tensor(lo.rearrange(flat), sums, hi.bitcast(F32).rearrange(flat),
                                  ALU.subtract).then_inc(done, 1)

            def evacuate0(t, p):
                dve.wait_ge(in1_hi_ready, 4 * t + p + 1)
                pair = slice(2 * p, 2 * p + 2)
                evacuate(bank[L0_BANK[p]][:, :], in1_hi[:, pair, :], in1_lo[:, pair, :], in1_lo_ready)

            def evacuate1(t, p):
                dve.wait_ge(in2_hi_ready, 8 * t + 2 * p + 2)
                for i in (2 * p, 2 * p + 1):
                    dve.scalar_tensor_tensor(
                        out=in2_lo[:, i, :], in0=bank[L1_BANK[p]][:, (i % 2) * TOKENS:(i % 2 + 1) * TOKENS],
                        scalar=bias_sb[:, i:i + 1], in1=in2_hi[:, i, :].bitcast(F32),
                        op0=ALU.add, op1=ALU.subtract).then_inc(in2_lo_ready, 1)

            def evacuate2(t, p):
                dve.wait_ge(in3_hi_ready, 4 * (t - 1) + p + 1)
                pair = slice(2 * p, 2 * p + 2)
                evacuate(bank[L2_BANK[p]][:, :], in03_hi[:, pair, :], in03_lo[:, pair, :], in3_lo_ready)

            def wide(a):
                return a.unsqueeze(2).to_broadcast([P, TT, EXPERTS])

            top, top_key, second, second_key, gap, e, g1, g2 = (stat[:, n, :] for n in range(8))

            def gate_steps(t, first):
                steps = [first]

                def step(ins):
                    steps[0] += 1
                    ins.then_inc(gate_step, 1)
                    dve.wait_ge(gate_step, GATE_STEPS * t + steps[0])

                return step

            def choose(t):
                step = gate_steps(t, 0)
                order = first_key[:, :].unsqueeze(1).to_broadcast([P, TT, EXPERTS])
                dve.wait_ge(down_done, t + 1)
                step(dve.tensor_tensor(rest[:, :, :], down_lo[:, :, ER:HL],
                                       lang_bias[:, bass.ds(t, 1), :].to_broadcast([P, TT, EXPERTS]), ALU.add))
                step(dve.tensor_tensor(logits[:, :, :], down_hi[:, :, ER:HL], rest[:, :, :], ALU.add))
                step(dve.tensor_reduce(top, logits[:, :, :], AX_X, ALU.max))
                step(dve.tensor_tensor(same[:, :, :], logits[:, :, :], wide(top), ALU.is_equal))
                step(dve.tensor_tensor(key[:, :, :], same[:, :, :], order, ALU.mult))
                step(dve.tensor_reduce(top_key, key[:, :, :], AX_X, ALU.max))
                step(dve.tensor_tensor(pick1[:, :, :], key[:, :, :], wide(top_key), ALU.is_equal))
                step(dve.scalar_tensor_tensor(out=rest[:, :, :], in0=pick1[:, :, :], scalar=LOWEST,
                                              in1=logits[:, :, :], op0=ALU.mult, op1=ALU.add))
                step(dve.tensor_reduce(second, rest[:, :, :], AX_X, ALU.max))
                step(dve.tensor_tensor(gap, second, top, ALU.subtract))
                step(dve.tensor_tensor(same[:, :, :], rest[:, :, :], wide(second), ALU.is_equal))
                step(dve.tensor_tensor(key[:, :, :], same[:, :, :], order, ALU.mult))
                step(dve.tensor_reduce(second_key, key[:, :, :], AX_X, ALU.max))
                step(dve.tensor_tensor(pick2[:, :, :], key[:, :, :], wide(second_key), ALU.is_equal))

            def gate(t):
                step = gate_steps(t, 14)
                dve.wait_ge(down_lo_copied, t + 1)
                step(dve.tensor_tensor(gated[:, :, :], down_hi[:, :, 0:ER], gated[:, :, :], ALU.add))
                dve.wait_ge(exp_ready, t + 1)
                step(dve.tensor_scalar(g1, e, 1.0, None, ALU.add))
                step(dve.reciprocal(g2, g1))
                step(dve.tensor_scalar(g1, g2, SCALING, None, ALU.mult))
                step(dve.tensor_tensor(g2, g1, e, ALU.mult))
                step(dve.tensor_tensor(pick1[:, :, :], pick1[:, :, :], wide(g1), ALU.mult))
                step(dve.tensor_tensor(pick2[:, :, :], pick2[:, :, :], wide(g2), ALU.mult))
                step(dve.tensor_tensor(gates[:, :, :], pick1[:, :, :], pick2[:, :, :], ALU.add))
                rank_cols = "p s (e r) -> p s e r"
                dve.tensor_tensor(gated[:, :, :].rearrange(rank_cols, r=RANK),
                                  gated[:, :, :].rearrange(rank_cols, r=RANK),
                                  gates[:, :, :].unsqueeze(3).to_broadcast([P, TT, EXPERTS, RANK]), ALU.mult
                                  ).then_inc(gated_ready, 1)

            def split_gated(t):
                dve.wait_ge(gatedT_hi_ready, t + 1)
                dve.tensor_tensor(gatedT_lo[:, :], gatedT_ps, gatedT_hi[:, :].bitcast(F32),
                                  ALU.subtract).then_inc(gatedT_lo_ready, 1)

            def take_coeff(t):
                dve.tensor_copy(coeff_now[:, :], coeff_pair[:, bass.ds(t, 1), :].rearrange("p b c -> p (b c)")
                                ).then_inc(coeff_ready, 1)

            def split_layer3(t):
                dve.wait_ge(b3_hi_ready, t)
                for r in range(REP):
                    op = dve.tensor_tensor(b3_split[:, :, r, 1, :], b3_raw[:, :, :],
                                           b3_split[:, :, r, 0, :].bitcast(F32), ALU.subtract)
                op.then_inc(b3_ready, 1)
                dve.wait_ge(a3_hi_ready, t)
                low = slice(4 * RANK, 6 * RANK)
                dve.tensor_tensor(a3_split[low, :], a3_raw[low, :], a3_split[low, :].bitcast(F32),
                                  ALU.subtract).then_inc(a3_ready, 1)

            def split_rank(t):
                dve.wait_ge(rank_hi_ready, t)
                low = slice(2 * RANK, 4 * RANK)
                dve.tensor_tensor(rank_rows[low, :], rank_ps[low, :], rank_rows[low, :].bitcast(F32),
                                  ALU.subtract).then_inc(rank_ready, 1)

            def layer1_phase(t, before, after):
                split_tile(t, 10)
                if before:
                    split_rank(t)
                split_tile(t, 11)
                if after:
                    split_x(t, 0)
                    split_x(t, 1)
                evacuate1(t, 0)
                split_tile(t, 12)
                split_tile(t, 13)
                evacuate1(t, 1)
                if after:
                    choose(t + 1)
                split_tile(t, 14)
                if after:
                    gate(t + 1)
                split_tile(t, 15)
                evacuate1(t, 2)
                split_tile(t, 16)
                if after:
                    split_gated(t + 1)
                evacuate1(t, 3)
                split_tile(t, 17)
                if after:
                    evacuate0(t + 1, 0)
                    evacuate0(t + 1, 1)

            def layer2_phase(t):
                take_coeff(t)
                split_layer3(t)
                split_tile(t, 2)
                split_tile(t, 3)
                evacuate0(t, 2)
                split_tile(t, 4)
                split_tile(t, 5)
                evacuate0(t, 3)
                evacuate2(t, 0)
                evacuate2(t, 1)
                split_tile(t, 6)
                split_tile(t, 7)
                evacuate2(t, 2)
                split_tile(t, 8)
                split_tile(t, 9)
                evacuate2(t, 3)

            def setup():
                steps = [0]

                def step(ins):
                    steps[0] += 1
                    ins.then_inc(setup_step, 1)
                    dve.wait_ge(setup_step, steps[0])

                dve.wait_ge(small_landed, 48)
                step(dve.tensor_copy(expert_no[:, :], expert_i[:, :]))
                step(dve.tensor_scalar(first_key[:, :], expert_no[:, :], -1.0, float(EXPERTS), ALU.mult, ALU.add))
                step(dve.tensor_copy(lang_f[:, :], lang_i[:, :]))
                shape = [P, BATCHES, EXPERTS]
                step(dve.tensor_tensor(lang_bias[:, :, :], lang_f[:, :].unsqueeze(2).to_broadcast(shape),
                                       expert_no[:, :].unsqueeze(1).to_broadcast(shape), ALU.is_equal))
                step(dve.tensor_scalar(lang_bias[:, :, :], lang_bias[:, :, :], LANG_BIAS, None, ALU.mult))
                step(dve.tensor_scalar(coeff_pair[:, :, 0], coeff_all[:, :], 2.0, None, ALU.mult))
                step(dve.tensor_scalar(coeff_pair[:, :, 1], coeff_all[:, :], -1.0, None, ALU.mult))

            flat = "p k c -> p (k c)"
            split_low(0, 0)
            for half in range(2):
                rows = slice(4 * half, 4 * half + 4)
                dve.wait_ge(x_hi_ready, half + 1)
                dve.tensor_tensor(in03_lo[:, rows, :].rearrange(flat), x0_raw[half],
                                  in03_hi[:, rows, :].bitcast(F32).rearrange(flat), ALU.subtract).then_inc(x_lo_ready, 1)
            split_low(0, 1)
            dve.wait_ge(awr_hi_ready, 2)
            dve.tensor_tensor(awr[:, :, 1, ER:HL], wr_raw[:, :, :], awr[:, :, 0, ER:HL].bitcast(F32), ALU.subtract)
            dve.tensor_tensor(awr[:, :, 1, 0:ER], a0_raw,
                              awr[:, :, 0, 0:ER].bitcast(F32), ALU.subtract).then_inc(awr_lo_ready, 1)
            setup()
            take_coeff(0)
            dve.wait_ge(consts_ready, 1)
            split_tile(0, 2)
            split_tile(0, 3)
            choose(0)
            split_tile(0, 4)
            gate(0)
            split_tile(0, 5)
            dve.wait_ge(b0_hi_ready, 1)
            dve.tensor_tensor(b0_lo[:, :], b0_raw, b0_hi[:, :].bitcast(F32), ALU.subtract).then_inc(b0_lo_ready, 1)
            split_gated(0)
            split_tile(0, 6)
            split_tile(0, 7)
            evacuate0(0, 0)
            evacuate0(0, 1)
            finish_raw(0, 9)
            evacuate0(0, 2)
            split_low(0, 8)
            evacuate0(0, 3)
            split_tile(0, 9)
            layer1_phase(0, False, True)

            with dve.Fori(1, BATCHES - 1) as t:
                layer2_phase(t)
                layer1_phase(t, True, True)
            layer2_phase(BATCHES - 1)
            layer1_phase(BATCHES - 1, True, False)

            split_layer3(BATCHES)
            for p in range(PAIRS):
                if p < PAIRS - 1:
                    split_tile(BATCHES, 2 * p + 2, last=True)
                    split_tile(BATCHES, 2 * p + 3, last=True)
                evacuate2(BATCHES, p)
            split_rank(BATCHES)
            for p in (1, 3):
                dve.wait_ge(l3_done, 4 * (BATCHES - 1) + p + 1)
                dve.tensor_copy(raw[:, p, 0:4, :].rearrange(flat), bank[L2_BANK[p]][:, :]).then_inc(last_staged, 1)


_OUT = (BATCHES, PAIRS, P, 2 * TOKENS)


def kernel(x, itok_B_0_7, condB_coeff, itok_B_3_7, mask_Bx4096x4096_ik1, L0_cond_W, L0_cond_Wr, L0_cond_A,
           L0_cond_B, L1_cond_W, L1_cond_b, L2_cond_weight, L3_cond_A, L3_cond_B):
    import numpy as np
    import concourse.bacc as bacc
    from concourse.bass_utils import run_bass_kernel_spmd

    def tiles(w):
        lead = w.shape[:-2]
        w = w.reshape(*lead, KT, P, OT, P)
        n = len(lead)
        w = w.transpose(*range(n), n + 2, n + 1, n, n + 3)
        return np.ascontiguousarray(w).reshape(*lead, OT, P, KT * P)

    def inputs_first(w, cols):
        return np.ascontiguousarray(w.reshape(KT, P, cols).transpose(1, 0, 2)).reshape(P, KT * cols)

    a = {k: np.asarray(v) for k, v in dict(
        x=x, lang=itok_B_0_7, coeff=condB_coeff, ids=itok_B_3_7, mask=mask_Bx4096x4096_ik1, w0=L0_cond_W,
        wr=L0_cond_Wr, a0=L0_cond_A, b0=L0_cond_B, w1=L1_cond_W, bias1=L1_cond_b, w2=L2_cond_weight,
        a3=L3_cond_A, b3=L3_cond_B).items()}
    arrays = {
        "x": np.ascontiguousarray(a["x"].reshape(BATCHES, TOKENS, 2, KT // 2, P).transpose(0, 2, 4, 3, 1)
                                  ).reshape(BATCHES, 2, P, KT // 2 * TOKENS),
        "lang_ids": a["lang"],
        "coeff": a["coeff"],
        "ids": a["ids"],
        "mask": tiles(a["mask"]),
        "w0": tiles(a["w0"].T),
        "wr": inputs_first(a["wr"].T, EXPERTS),
        "a0": inputs_first(a["a0"].reshape(ER, D).T, ER),
        "b0": np.ascontiguousarray(a["b0"].transpose(0, 2, 1)).reshape(ER, D),
        "w1": tiles(a["w1"].T),
        "bias1": np.ascontiguousarray(a["bias1"].reshape(OT, P).T),
        "w2": tiles(a["w2"].transpose(0, 2, 1)),
        "a3": np.ascontiguousarray(a["a3"].transpose(0, 2, 1)),
        "b3": np.ascontiguousarray(a["b3"].reshape(EXPERTS, RANK, KT, P).transpose(0, 3, 2, 1)
                                   ).reshape(EXPERTS, P, KT * RANK),
    }
    nc = bacc.Bacc("TRN2", target_bir_lowering=False, num_devices=1, dynamic_dma_scratch_size=1024)
    args = [nc.dram_tensor(f"in_{name}", v.shape, mybir.dt.from_np(v.dtype), kind="ExternalInput").ap()
            for name, v in arrays.items()]
    out = nc.dram_tensor("out_0", _OUT, F32, kind="ExternalOutput").ap()
    cond_resid_kernel(nc, *args, out)
    got = run_bass_kernel_spmd(nc, [{f"in_{n}": v for n, v in arrays.items()}], core_ids=[0])
    y = got.results[0]["out_0"].reshape(BATCHES, PAIRS, P, 2, TOKENS)
    return np.ascontiguousarray(y.transpose(0, 4, 1, 3, 2)).reshape(BATCHES, TOKENS, D)
```
